# Optimizing a Trainium2 kernel written in Bass

```python
import numpy as np
import jax
import jax.numpy as jnp

def _softmax(x, axis=-1):
    return jax.nn.softmax(x, axis=axis)
def _gelu(x):
    return jax.nn.gelu(x, approximate=True)
def _silu(x):
    return jax.nn.silu(x)
def _sigmoid(x):
    return jax.nn.sigmoid(x)
def _layernorm(x, axis=-1, eps=1e-5):
    m = jnp.mean(x, axis=axis, keepdims=True)
    v = jnp.var(x, axis=axis, keepdims=True)
    return (x - m) / jnp.sqrt(v + eps)
def _scatter_add(tgt, idx, src, axis=0):
    return tgt.at[idx].add(src)
def _segment_sum(src, seg, n):
    return jax.ops.segment_sum(src, seg, n)

kernel_name = 'mk_adj_preln_d1_adj_512_b7adfb'

def setup_inputs(seed: int = 0):
    np.random.seed(seed)
    _w = jnp.asarray
    def _rec_inputs():
        import jax
        import jax.numpy as jnp
        _gk = jax.random.key(seed)
        x = -0.0002928 + 1 * jax.random.normal(jax.random.fold_in(_gk, 1), (2708, 512), jnp.float32)
        _a = jax.random.bernoulli(jax.random.fold_in(_gk, 2), 0.0118168, (2708, 2708))
        _a = jnp.logical_or(_a, jnp.swapaxes(_a, -1, -2))
        _a = jnp.logical_or(_a, jnp.eye(2708, dtype=bool))
        _af = _a.astype(jnp.float32)
        _af = _af * jax.random.uniform(jax.random.fold_in(_gk, 3), (2708, 2708), jnp.float32, 0.05, 1)
        adj = _af
        return x, adj
    x, adj = _rec_inputs()
    def _L0_gnn_setup():
        import jax, jax.numpy as jnp
        import numpy as np
        N, NFEAT, NHID = (8192, 512, 1024)

        def _gc(x, adj, W, b):
            return adj @ (x @ W) + b
        key = jax.random.key(seed)
        ks = jax.random.split(key, 8)

        def glorot(k, shape):
            bound = 1.0 / np.sqrt(shape[0])
            return jax.random.uniform(k, shape, jnp.float32, -bound, bound)
        return {'x': jax.random.normal(ks[0], (N, NFEAT), jnp.float32), 'adj': jax.random.uniform(ks[1], (N, N), jnp.float32), 'W1': glorot(ks[2], (NFEAT, NHID)), 'b1': glorot(ks[3], (NHID,)), 'W2': glorot(ks[4], (NHID, NHID)), 'b2': glorot(ks[5], (NHID,)), 'W3': glorot(ks[6], (NHID, NFEAT)), 'b3': glorot(ks[7], (NFEAT,))}
    _L0_gnn_all = _L0_gnn_setup()
    _L0_gnn_in = {k: v for k, v in _L0_gnn_all.items() if k in ('W1', 'b1', 'W2', 'b2', 'W3', 'b3', )}
    del _L0_gnn_all

    return {
        "x": x,
        "adj": adj,
        "L0_gnn_W1": _L0_gnn_in["W1"],
        "L0_gnn_b1": _L0_gnn_in["b1"],
        "L0_gnn_W2": _L0_gnn_in["W2"],
        "L0_gnn_b2": _L0_gnn_in["b2"],
        "L0_gnn_W3": _L0_gnn_in["W3"],
        "L0_gnn_b3": _L0_gnn_in["b3"],
    }

def reference(x, adj, L0_gnn_W1, L0_gnn_b1, L0_gnn_W2, L0_gnn_b2, L0_gnn_W3, L0_gnn_b3):
    import jax
    import jax.numpy as jnp
    def _L0_gnn_ref(x, adj, W1, b1, W2, b2, W3, b3):
        import jax, jax.numpy as jnp
        import numpy as np
        N, NFEAT, NHID = (8192, 512, 1024)

        def _gc(x, adj, W, b):
            return adj @ (x @ W) + b
        h = jax.nn.relu(_gc(x, adj, W1, b1))
        h = jax.nn.relu(_gc(h, adj, W2, b2))
        return _gc(h, adj, W3, b3)

    h = jnp.maximum(_layernorm(x, axis=-1), 0.0)
    x = x + _L0_gnn_ref(h, adj, L0_gnn_W1, L0_gnn_b1, L0_gnn_W2, L0_gnn_b2, L0_gnn_W3, L0_gnn_b3)
    return x


_drawn_inputs = setup_inputs


def setup_inputs(seed=0):
    import zlib

    import numpy as np

    out = dict(_drawn_inputs(seed))
    spreads = {}
    factors = {'L0_gnn_b1': 29.652, 'L0_gnn_b2': 200.0, 'L0_gnn_b3': 200.0}
    for name, (base, spread) in spreads.items():
        noise = np.random.default_rng([zlib.crc32(name.encode()), seed]).standard_normal(out[name].shape)
        drawn = base * np.exp(spread * noise) if base else spread * noise
        out[name] = jnp.asarray(drawn.astype(out[name].dtype))
    for name, factor in factors.items():
        out[name] = (out[name] * factor).astype(out[name].dtype)
    return out
```

```python
from contextlib import ExitStack

import concourse.bass as bass
from concourse import mybir

F32 = mybir.dt.float32
F32R = mybir.dt.float32r
ALU = mybir.AluOpType
ACT = mybir.ActivationFunctionType

P = 128
BANK = 512
RING = 7
RAW = 3
HEAD = 4
LATE = 4
STAGES = 4
STEP = 32
EPS = 1e-5



class Job:

    def __init__(self, kind, cut, chunk=0, tile=0, col=0, width=0, half=None, source=None):
        self.kind, self.cut, self.ready = kind, cut, cut + 1
        self.chunk, self.tile, self.col, self.width, self.half, self.source = chunk, tile, col, width, half, source
        self.raw = self.raw_freed = self.tail_use = self.slot = self.acc_before = self.slot_before = None
        self.partner = None
        self.cut_x = self.root = self.steps = None


class Drain:

    def __init__(self, number, bank, part, tile):
        self.number, self.bank, self.part, self.tile = number, bank, part, tile
        self.done = self.bank_free = self.on_slot = None
        self.stage = self.stage_free = self.stored = None
        self.still_hi = self.still = self.rep = 0


class Unit:

    def __init__(self, phase, index, col=0, width=0):
        self.phase, self.index, self.col, self.width = phase, index, col, width
        self.jobs, self.drains, self.tiles, self.blocks, self.after = [], [], [], [], []


def plan(N, F, H):
    NT, TAIL = N // P, N % P
    blocks = [4, 4, 4, 4, 3, NT - 19]
    chunks, col = [], 0
    for n in blocks:
        width = n * P + (TAIL if n == blocks[-1] and len(chunks) == len(blocks) - 1 else 0)
        chunks.append((col, width))
        col += width
    assert col == N and max(w for _, w in chunks) <= BANK
    now = {"cut": 0, "raw": 0, "slot": 0, "acc": 0, "drain": 0, "still_hi": 0, "still": 0, "tail": 0, "rep": 0}
    raw_user, tail_user = [None] * RAW, [None]
    stored, bank_drained = [0] * STAGES, [None] * 8
    units = {}

    def job(kind, ring=None, raw=True, **more):
        j = Job(kind, now["cut"], **more)
        now["cut"] += 1
        if raw is True:
            j.raw = now["raw"]
            before = raw_user[j.raw % RAW]
            j.raw_freed = before.cut + 1 if before else None
            raw_user[j.raw % RAW] = j
            now["raw"] += 1
        if raw == "tail":
            j.raw_freed = tail_user[0].cut + 1 if tail_user[0] else None
            tail_user[0] = j
            now["tail"] += 1
            j.tail_use = now["tail"]
        if ring:
            j.slot = now["slot"]
            now["slot"] += 1
        else:
            j.acc_before = now["acc"] or None
        return j

    def drain(bank, on_slot=None, stores=0, part=0, tile=0):
        d = Drain(now["drain"], bank, part, tile)
        d.on_slot = on_slot
        now["drain"] += 1
        if on_slot is None:
            now["acc"] += 1
            d.done = now["acc"]
        else:
            d.done = on_slot + 1
        d.bank_free = bank_drained[bank]
        bank_drained[bank] = d.number + 1
        if stores:
            d.stage = part % STAGES
            d.stage_free = 16 * stored[d.stage] or None
            stored[d.stage] += stores
            d.stored = 16 * stored[d.stage]
        return d

    def adj_pass(name, weights, store, extra=None):
        us = []
        for c, (col, width) in enumerate(chunks):
            u = Unit(name, c, col, width)
            for t in range(NT):
                u.jobs.append(job("adj", ring=True, chunk=c, tile=t, col=col, width=width))
                if name == "pass1" and c == 0:
                    u.jobs.append(job("x", raw=False, tile=t))
                    u.jobs[-2].ready, u.jobs[-2].partner = u.jobs[-1].ready, u.jobs[-1]
                    if t == 5:
                        u.jobs.append(job("x", raw="tail", tile=NT))
                for w in weights.get((c, t), ()):
                    u.jobs.append(job("weight", source=w))
            u.jobs.append(job("adj", raw="tail", chunk=c, tile=NT, col=col, width=width))
            u.tiles = [j for j in u.jobs if j.kind == "adj"]
            u.drains = [drain(b, part=b, stores=store) for b in range(F // P)]
            us.append(u)
        units[name] = us

    def block_phase(name, slots_per_block, blocks_per_unit=7):
        us = []
        for g in range(NT // blocks_per_unit):
            u = Unit(name, g)
            last = g == NT // blocks_per_unit - 1
            for p in range(blocks_per_unit + last):
                b = g * blocks_per_unit + p
                short = b == NT
                w = TAIL if short else P
                raw = name == "w3"
                if short:
                    js = [job(name, raw=raw, tile=b, width=w, half=None)]
                else:
                    js = [job(name, raw=raw, ring=True, tile=b, width=w, half=h) for h in range(slots_per_block)]
                u.jobs += js
                d = drain(p, on_slot=None if short else js[-1].slot, tile=b)
                now["still_hi"] += 1
                d.still_hi = now["still_hi"]
                d.rep = 0
                if short:
                    now["rep"] += 1
                    d.rep = now["rep"]
                if short or name != "w3":
                    now["still"] += 1
                d.still = now["still"]
                u.blocks.append((b, p, js, d))
                u.drains.append(d)
            us.append(u)
        units[name] = us

    def w2_phase():
        us = []
        for c, (col, width) in enumerate(chunks):
            u = Unit("w2", c, col, width)
            for k in range(H // P):
                u.jobs.append(job("p2", ring=k < RING, chunk=c, tile=k, col=col, width=width))
            u.tiles = list(u.jobs)
            if c == len(chunks) - 1:
                for k in range(H // P):
                    w = job("weight", source=("W3", k, 0))
                    w.acc_before, w.slot_before = None, u.tiles[3].slot + 1
                    u.jobs.append(w)
            u.drains = [drain(m, part=m, stores=2 if width % P else 1) for m in range(H // P)]
            us.append(u)
        units["w2"] = us

    KF, KH = F // P, H // P
    adj_pass("pass1", {(4, 5 + 2 * k): [("W1", k, 0)] for k in range(KF)}, 0)
    w1_ready = {0: units["pass1"][4].jobs[-1].cut}
    block_phase("h1a", 1)
    adj_pass("pass2a", {(4, 5 + 2 * k): [("W1", k, 1)] for k in range(KF)}, 1)
    w1_ready[1] = units["pass2a"][4].jobs[-1].cut
    block_phase("h1b", 1)
    adj_pass("pass2b", {(4 + k // 4, 5 + 2 * (k % 4)): [("W2", k, 0), ("W2", k, 1)] for k in range(KH)}, 1)
    w2_phase()
    block_phase("w3", 2)
    adj_pass("pass3", {}, 1)
    order = ["pass1", "h1a", "pass2a", "h1b", "pass2b", "w2", "w3", "pass3"]
    flat = [u for name in order for u in units[name]]
    for u, v in zip(flat, flat[1:]):
        u.after = v.jobs
    flat[-1].after = []
    return units, chunks, order, w1_ready, [16 * s for s in stored]


def exact(values, i):
    step = values[1] - values[0] if len(values) > 1 else 0
    assert all(v == values[0] + k * step for k, v in enumerate(values))
    return values[0] + i * step if step else values[0]


def count(values, i):
    step = values[-1] - values[-2] if len(values) > 1 else 0
    least = max(v - k * step for k, v in enumerate(values) if v is not None)
    assert least > 0
    return least + i * step if step else least


def gcn_kernel(nc, x, xT, adjT, W1, W2, W3, b1, b2T, b3T, outT, P2, H2, H2tail):
    N, F = x.shape
    H = W1.shape[1]
    NT, TAIL = N // P, N % P
    KF, KH = F // P, H // P
    REP = 2 * STEP + TAIL
    units, chunks, order, w1_ready, stored_all = plan(N, F, H)
    PASSES = ("pass1", "pass2a", "pass2b", "pass3")

    at = nc.sbuf_base + (-nc.sbuf_base) % 64

    def place(name, shape, dtype, offset=None):
        nonlocal at
        here = at if offset is None else offset
        size = 4
        for n in shape[1:]:
            size *= n
        if offset is None:
            at += size + (-size) % 64
        assert here + size <= nc.sbuf_usable_end
        return nc.alloc_sbuf_tensor_at(name, shape, dtype, offset=here)

    still_hi = place("still_hi", [P, NT, F], F32R)
    still_lo = place("still_lo", [P, NT, F], F32R)
    still_tail = place("still_tail", [P, F], F32R)
    slot_hi = place("slot_hi", [P, RING, BANK], F32R)
    slot_lo = place("slot_lo", [P, RING, BANK], F32R)
    slot_tail = place("slot_tail", [P, BANK], F32R)
    raw = place("raw", [P, RAW, BANK], F32)
    raw_tail = place("raw_tail", [P, BANK], F32)
    stage = place("stage", [P, STAGES, BANK], F32)
    rep = place("rep", [P, F], F32)
    b1_rows = place("b1_rows", [P, H], F32)
    b2_cols = place("b2_cols", [P, KH], F32)
    b3_cols = place("b3_cols", [P, KF], F32)
    stats = place("stats", [P, 6], F32)
    moments = place("moments", [P, 2 * (NT + 1)], F32)
    spread = place("spread", [P, 6 * (NT + 1)], F32)
    region = at
    P1 = place("P1", [P, KF, N], F32)
    W1_hi = place("W1_hi", [P, KF, BANK], F32R)
    W1_lo = place("W1_lo", [P, KF, BANK], F32R)
    W2_hi = place("W2_hi", [P, KH, H], F32R, region)
    W2_lo = place("W2_lo", [P, KH, H], F32R, region + KH * H * 4)
    W3_hi = place("W3_hi", [P, KH, F], F32R, region)
    W3_lo = place("W3_lo", [P, KH, F], F32R, region + KH * H * 4)
    x_cols = place("x_cols", [P, KF, BANK], F32, region)
    extra_hi = still_hi[:, NT - 1, :]
    extra_lo = still_lo[:, NT - 1, :]

    with ExitStack() as ctx:
        def sem(name):
            return ctx.enter_context(nc.semaphore(name))

        ps = ctx.enter_context(nc.psum_tensor("ps", [P, 8, BANK], F32))

        zeroed = sem("zeroed")
        biases_in = sem("biases_in")
        raw_in = [sem(f"raw_in{r}") for r in range(RAW)]
        tail_in = sem("tail_in")
        x_in = [sem(f"x_in{s}") for s in range(STAGES)]
        xT_in = [sem(f"xT_in{b}") for b in range(KF)]
        rep_in = sem("rep_in")
        ln_step = sem("ln_step")
        root_done = sem("root_done")
        ln_done = sem("ln_done")
        hi_done = sem("hi_done")
        lo_done = sem("lo_done")
        slot_used = sem("slot_used")
        acc_done = sem("acc_done")
        drained = sem("drained")
        still_hi_done = sem("still_hi_done")
        still_done = sem("still_done")
        stored = [sem(f"stored{s}") for s in range(STAGES)]

        block = ctx.enter_context(nc.Block())

        def cut_parts(js):
            j = js[0]
            if j.kind == "weight":
                name, k, half = j.source
                cols = slice(half * BANK, half * BANK + BANK) if name == "W2" else slice(0, BANK)
                hi, lo = {"W1": (W1_hi, W1_lo), "W2": (W2_hi, W2_lo), "W3": (W3_hi, W3_lo)}[name]
                return hi[:, k, cols], lo[:, k, cols], raw[:, j.raw % RAW, :]
            if j.kind == "h1a" or j.kind == "h1b":
                if j.slot is None:
                    w = KF * TAIL
                    return (slot_tail[:, 0:w].rearrange("p (k i) -> p k i", k=KF),
                            slot_tail[:, BANK // 2:BANK // 2 + w].rearrange("p (k i) -> p k i", k=KF),
                            P1[:, :, NT * P:N])
                return (slot_hi[:, j.slot % RING, :].rearrange("p (k i) -> p k i", k=KF),
                        slot_lo[:, j.slot % RING, :].rearrange("p (k i) -> p k i", k=KF), None)
            if j.kind == "w3" and j.slot is None:
                w = KH * TAIL
                return slot_tail[:, 0:w], slot_tail[:, BANK // 2:BANK // 2 + w], raw[:, j.raw % RAW, 0:w]
            if j.kind == "w3":
                return slot_hi[:, j.slot % RING, :], slot_lo[:, j.slot % RING, :], raw[:, j.raw % RAW, :]
            w = j.width
            if j.kind == "p2" and j.slot is None:
                return extra_hi[:, 0:w], extra_lo[:, 0:w], raw[:, j.raw % RAW, 0:w]
            return slot_hi[:, j.slot % RING, 0:w], slot_lo[:, j.slot % RING, 0:w], raw[:, j.raw % RAW, 0:w]

        def source_of(js, i):
            hi, lo, src = cut_parts(js)
            if src is None:
                src = P1[:, :, bass.ds(exact([j.tile for j in js], i) * P, P)]
            return hi, lo, src

        first_x = [j for j in units["pass1"][0].jobs if j.kind == "x"]
        x_jobs = [j for j in first_x if j.tail_use is None]
        stats_order = [x_jobs[0]]
        for j in first_x:
            stats_order += [j] if j.tail_use is not None else x_jobs[j.tile + 1:j.tile + 2]
        for n, j in enumerate(stats_order):
            j.root = n + 1
        for n, j in enumerate(first_x):
            j.cut_x = n
        n = 0
        for j in first_x:
            if j is first_x[0]:
                n += 3
                j.steps = n
            ahead_of = j if j.tail_use is not None else (x_jobs + [None])[j.tile + 1]
            if ahead_of is not None:
                n += 3
                ahead_of.steps = n
            n += 4

        @block.sync
        def _(sp):
            def load(js, i):
                j = js[0]
                if j.kind in ("h1a", "h1b"):
                    return
                if j.kind == "x" and j.tail_use is None:
                    s = j.tile % STAGES
                    if j.tile >= STAGES:
                        sp.wait_ge(lo_done, x_jobs[j.tile - STAGES].cut + 1)
                    sp.dma_start(stage[:, s, :], x[j.tile * P:(j.tile + 1) * P, :]).then_inc(x_in[s], 16)
                    return
                if j.raw_freed is not None:
                    sp.wait_ge(lo_done, count([q.raw_freed for q in js], i))
                if j.tail_use is not None:
                    src = x[NT * P:N, :] if j.kind == "x" else \
                        adjT[NT * P:N, bass.ds(exact([q.col for q in js], i), j.width)]
                    w = F if j.kind == "x" else j.width
                    for r in range(3):
                        sp.dma_start(raw_tail[r * STEP:r * STEP + TAIL, 0:w], src).then_inc(tail_in, 16)
                    return
                r = j.raw % RAW
                if j.kind == "weight":
                    name, k, half = j.source
                    w = {"W1": W1, "W2": W2, "W3": W3}[name]
                    sp.dma_start(raw[:, r, :], w[k * P:(k + 1) * P, half * BANK:half * BANK + BANK]) \
                        .then_inc(raw_in[r], 16)
                elif j.kind == "adj":
                    sp.dma_start(raw[:, r, 0:j.width],
                                 adjT[j.tile * P:(j.tile + 1) * P, bass.ds(exact([q.col for q in js], i), j.width)]) \
                        .then_inc(raw_in[r], 16)
                elif j.kind == "p2":
                    made = [units["pass2a" if q.tile < KF else "pass2b"][q.chunk].drains[q.tile % KF] for q in js]
                    sp.wait_ge(stored[made[0].stage], count([d.stored for d in made], i))
                    sp.dma_start(raw[:, r, 0:j.width], P2[j.tile, :, bass.ds(exact([q.col for q in js], i), j.width)]) \
                        .then_inc(raw_in[r], 16)
                elif j.slot is None:
                    for s in range(STAGES):
                        sp.wait_ge(stored[s], units["w2"][-1].drains[KH - STAGES + s].stored)
                    sp.dma_start(raw[:, r, 0:KH * TAIL], H2tail.rearrange("p k i -> p (k i)")).then_inc(raw_in[r], 16)
                else:
                    made = [units["w2"][min(q.tile // 4, 4) if q.tile < 19 else 5] for q in js]
                    for s in range(STAGES):
                        need = [u.drains[KH - STAGES + s].stored for u in made]
                        sp.wait_ge(stored[s], need[0] if len(need) == 1 else count([max(need)] * 2, 0))
                    b = exact([q.tile for q in js], i)
                    half = KH // 2 * P
                    sp.dma_start(raw[:, r, :], H2[bass.ds(b * P, P), j.half * half:(j.half + 1) * half]) \
                        .then_inc(raw_in[r], 16)

            def load_xT(us, i):
                for b in range(KF):
                    if us[0].index == 0:
                        sp.wait_ge(acc_done, units["w3"][-1].drains[-1].done)
                    else:
                        sp.wait_ge(drained, count([units["pass3"][u.index - 1].drains[b].number + 1 for u in us], i))
                    sp.dma_start(x_cols[:, b, 0:us[0].width],
                                 xT[b * P:(b + 1) * P, bass.ds(exact([u.col for u in us], i), us[0].width)]) \
                        .then_inc(xT_in[b], 16)

            def unit_loads(us, i):
                for q, j in enumerate(us[0].jobs):
                    if us[0].phase == "pass3" and q == 12:
                        load_xT(us, i)
                    load([u.jobs[q] for u in us], i)

            sp.dma_start(b1_rows[:, :], b1.partition_broadcast(P)).then_inc(biases_in, 16)
            sp.dma_start(b2_cols[:, :], b2T).then_inc(biases_in, 16)
            sp.dma_start(b3_cols[:, :], b3T).then_inc(biases_in, 16)
            first = units["pass1"][0].jobs
            sp.wait_ge(zeroed, 2)
            for j in first:
                if j.partner is not None:
                    load([j.partner], 0)
                    load([j], 0)
                elif j.tail_use is not None:
                    load([j], 0)
            for name in order:
                us = units[name]
                if name in ("h1a", "h1b"):
                    continue
                if name == "pass1":
                    groups = [us[1:4], us[4:5], us[5:6]]
                elif name == "pass3":
                    groups = [us[0:1], us[1:4], us[4:5], us[5:6]]
                elif name == "w3":
                    groups = [us[0:1], us[1:2], us[2:3]]
                elif name == "w2":
                    groups = [[u] for u in us]
                else:
                    groups = [us[0:4], us[4:5], us[5:6]]
                for g in groups:
                    if len(g) == 1:
                        unit_loads(g, 0)
                    else:
                        with sp.Fori(0, len(g)) as i:
                            unit_loads(g, i)
            for s in range(STAGES):
                sp.wait_ge(stored[s], stored_all[s])

        def cut_hi(act, js, i):
            j = js[0]
            if j.kind == "x":
                act.wait_ge(ln_done, (j.cut_x) + 1)
                if j.tail_use is None:
                    act.activation(still_hi[:, j.tile, :], stage[:, j.tile % STAGES, :], ACT.Relu).then_inc(hi_done, 1)
                else:
                    act.activation(still_tail[0:REP, :], raw_tail[0:REP, :], ACT.Relu).then_inc(hi_done, 1)
                return
            if j.raw is not None:
                act.wait_ge(raw_in[j.raw % RAW], count([16 * (q.raw // RAW + 1) for q in js], i))
            if j.tail_use is not None:
                act.wait_ge(tail_in, count([48 * q.tail_use for q in js], i))
            if j.slot is not None and j.slot >= RING:
                act.wait_ge(slot_used, count([q.slot - RING + 1 for q in js], i))
            elif j.kind == "weight" and j.source[0] == "W3":
                act.wait_ge(slot_used, j.slot_before)
            elif j.acc_before is not None:
                act.wait_ge(acc_done, count([q.acc_before for q in js], i))
            if j.kind in ("h1a", "h1b"):
                made = [units["pass1"][min(q.tile // 4, 4) if q.tile < 19 else 5].drains[-1].number + 1 for q in js]
                if j.kind == "h1a":
                    act.wait_ge(drained, max(made))
            if j.kind == "adj" and j.tail_use is not None:
                act.copy(slot_tail[0:REP, 0:j.width], raw_tail[0:REP, 0:j.width]).then_inc(hi_done, 1)
                return
            hi, lo, src = source_of(js, i)
            act.copy(hi, src).then_inc(hi_done, 1)

        def cut_lo(dve, js, i):
            j = js[0]
            dve.wait_ge(hi_done, count([q.cut + 1 for q in js], i))
            if j.kind == "x" and j.tail_use is None:
                dve.scalar_tensor_tensor(still_lo[:, j.tile, :], stage[:, j.tile % STAGES, :], 0.0,
                                         still_hi[:, j.tile, :].bitcast(F32), ALU.max, ALU.subtract) \
                    .then_inc(lo_done, 1)
            elif j.kind == "x":
                rows = slice(STEP, STEP + TAIL)
                dve.scalar_tensor_tensor(still_tail[rows, :], raw_tail[rows, :], 0.0,
                                         still_tail[rows, :].bitcast(F32), ALU.max, ALU.subtract) \
                    .then_inc(lo_done, 1)
            elif j.kind == "adj" and j.tail_use is not None:
                rows = slice(2 * STEP, REP)
                dve.tensor_tensor(slot_tail[rows, 0:j.width], raw_tail[rows, 0:j.width],
                                  slot_tail[rows, 0:j.width].bitcast(F32), ALU.subtract).then_inc(lo_done, 1)
            else:
                hi, lo, src = source_of(js, i)
                dve.tensor_tensor(lo, src, hi.bitcast(F32), ALU.subtract).then_inc(lo_done, 1)

        def chunk_groups(name, us):
            if name == "w2":
                return [[u] for u in us]
            if name == "pass2b":
                return [us[0:3], us[3:4], us[4:5], us[5:6]]
            return [us[0:1], us[1:3], us[3:4], us[4:5], us[5:6]]

        def ahead(us, q):
            return [(u.jobs + u.after)[q] if q < len(u.jobs) + len(u.after) else None for u in us]

        def run_cuts_and_drains(eng, cut, drain, finish):
            for name in order:
                us = units[name]
                if name in PASSES or name == "w2":
                    for g in chunk_groups(name, us):
                        def body(i):
                            n = len(g[0].jobs)
                            begin = 0 if (name == "pass1" and g[0].index == 0) else HEAD
                            for q in range(begin, n + (HEAD if g[0].after else 0)):
                                cut(eng, ahead(g, q), i)
                            for b in range(len(g[0].drains)):
                                drain(eng, [u.drains[b] for u in g], i, g[0])
                        if len(g) == 1:
                            body(0)
                        else:
                            with eng.Fori(0, len(g)) as i:
                                body(i)
                else:
                    per = 2 if name == "w3" else 1
                    for g in ([us[0:2], us[2:3]] if name != "w3" else [[u] for u in us]):
                        def body(i):
                            q = HEAD
                            n = len(g[0].jobs)
                            nb = len(g[0].blocks)
                            for p in range(nb):
                                upto = n + HEAD if p == nb - 1 else min(HEAD + per * (p + 1), n + HEAD)
                                while q < upto:
                                    cut(eng, ahead(g, q), i)
                                    q += 1
                                drain(eng, [u.drains[p] for u in g], i, g[0])
                            finish(eng, g, i)
                        if len(g) == 1:
                            body(0)
                        else:
                            with eng.Fori(0, len(g)) as i:
                                body(i)

        def result_done(eng, ds, i):
            eng.wait_ge(acc_done if ds[0].on_slot is None else slot_used, count([d.done for d in ds], i))

        T_OF = [0, 1, 0, 1, 0, 1, 2]

        @block.scalar
        def _(act):
            def drain(act, ds, i, u):
                d = ds[0]
                if u.phase == "pass1":
                    return
                if u.phase in ("h1a", "h1b", "w3"):
                    short = d.tile == NT
                    if short:
                        act.wait_ge(drained, d.number + 1)
                        for r in (1, 2):
                            act.dma_start(rep[r * STEP:r * STEP + TAIL, :], rep[0:TAIL, :]).then_inc(rep_in, 16)
                        act.wait_ge(rep_in, 32 * d.rep)
                        act.activation(still_tail[0:REP, :], rep[0:REP, :],
                                       ACT.Copy if u.phase == "w3" else ACT.Relu).then_inc(still_hi_done, 1)
                        return
                    tile = exact([q.tile for q in ds], i)
                    if u.phase == "w3":
                        result_done(act, ds, i)
                        act.copy(still_hi[:, bass.ds(tile, 1), :], ps[:, d.bank:d.bank + 1, :]) \
                            .then_inc(still_hi_done, 1)
                    else:
                        act.wait_ge(drained, count([q.number + 1 for q in ds], i))
                        t = T_OF[d.bank]
                        act.activation(still_hi[:, bass.ds(tile, 1), :], stage[:, t:t + 1, :], ACT.Relu) \
                            .then_inc(still_hi_done, 1)
                    return
                act.wait_ge(drained, count([q.number + 1 for q in ds], i))
                w = u.width
                group = unit_of(u, ds)
                col = exact([v.col for v in group], i)
                s = d.stage
                if u.phase == "pass3":
                    act.dma_start(outT[d.part * P:(d.part + 1) * P, bass.ds(col, w)], stage[:, s, 0:w]) \
                        .then_inc(stored[s], 16)
                elif u.phase == "w2":
                    full = w // P
                    b0 = u.col // P
                    act.dma_start(H2[b0 * P:(b0 + full) * P, d.part * P:(d.part + 1) * P]
                                  .rearrange("(b p) i -> p b i", p=P),
                                  stage[:, s, 0:full * P].rearrange("p (b i) -> p b i", i=P)).then_inc(stored[s], 16)
                    if w % P:
                        act.dma_start(H2tail[:, d.part, :], stage[:, s, full * P:w]).then_inc(stored[s], 16)
                else:
                    k = d.part + (KF if u.phase == "pass2b" else 0)
                    act.dma_start(P2[k, :, bass.ds(col, w)], stage[:, s, 0:w]).then_inc(stored[s], 16)

            def root(j):
                act.wait_ge(ln_step, j.steps)
                rows, c = slice(0, REP if j.tail_use is not None else P), 6 * j.cut_x
                act.activation(spread[rows, c + 1:c + 2], spread[rows, c:c + 1], ACT.Sqrt).then_inc(root_done, 1)

            def cut(act, js, i):
                j = js[0]
                if j.partner is not None:
                    x = j.partner
                    if x.tile == 0:
                        root(x)
                    if x.tile + 1 < NT:
                        root(x_jobs[x.tile + 1])
                elif j.kind == "x" and j.tail_use is not None:
                    root(j)
                cut_hi(act, js, i)

            def unit_of(u, ds):
                return units[u.phase][u.index:u.index + len(ds)]

            run_cuts_and_drains(act, cut, drain, lambda *a: None)

        @block.vector
        def _(dve):
            dve.memset(raw_tail[:, :], 0.0).then_inc(zeroed, 1)
            dve.memset(rep[:, :], 0.0).then_inc(zeroed, 1)
            steps = [0]

            def rows_of(j):
                short = j.tail_use is not None
                tile = raw_tail[0:REP, :] if short else stage[:, j.tile % STAGES, :]
                return tile, slice(0, REP if short else P), 2 * j.cut_x, 6 * j.cut_x

            def step(instruction):
                instruction.then_inc(ln_step, 1)
                steps[0] += 1
                dve.wait_ge(ln_step, steps[0])

            def statistics(j):
                tile, rows, m, c = rows_of(j)
                if j.tail_use is not None:
                    dve.wait_ge(tail_in, 48 * j.tail_use)
                else:
                    dve.wait_ge(x_in[j.tile % STAGES], 16 * (j.tile // STAGES + 1))
                step(dve.bn_stats(stats[rows, :], tile))
                step(dve.bn_aggr(moments[rows, m:m + 2], stats[rows, :]))
                dve.tensor_scalar(spread[rows, c:c + 1], moments[rows, m + 1:m + 2], EPS, None, ALU.add) \
                    .then_inc(ln_step, 1)
                steps[0] += 1

            def normalise(j):
                tile, rows, m, c = rows_of(j)
                v, root, r, e, f, rr = (spread[rows, c + k:c + k + 1] for k in range(6))
                dve.wait_ge(root_done, j.root)
                step(dve.reciprocal(r, root))
                step(dve.scalar_tensor_tensor(e, v, r, r, ALU.mult, ALU.mult))
                step(dve.tensor_scalar(f, e, -0.5, 1.5, ALU.mult, ALU.add))
                step(dve.tensor_tensor(rr, r, f, ALU.mult))
                dve.tensor_scalar(tile, tile, moments[rows, m:m + 1], rr, ALU.subtract, ALU.mult) \
                    .then_inc(ln_done, 1)

            def cut(dve, js, i):
                j = js[0]
                if j.partner is not None:
                    x = j.partner
                    if x.tile == 0:
                        statistics(x)
                    if x.tile + 1 < NT:
                        statistics(x_jobs[x.tile + 1])
                    normalise(x)
                elif j.kind == "x" and j.tail_use is not None:
                    statistics(j)
                    normalise(j)
                cut_lo(dve, js, i)

            def still_lo_part(g, p, i):
                ds = [u.drains[p] for u in g]
                d = ds[0]
                dve.wait_ge(still_hi_done, count([q.still_hi for q in ds], i))
                if d.tile == NT:
                    rows = slice(STEP, STEP + TAIL)
                    dve.scalar_tensor_tensor(still_tail[rows, :], rep[rows, :], 0.0, still_tail[rows, :].bitcast(F32),
                                             ALU.max, ALU.subtract).then_inc(still_done, 1)
                    return
                tile = exact([q.tile for q in ds], i)
                t = T_OF[d.bank]
                dve.scalar_tensor_tensor(still_lo[:, bass.ds(tile, 1), :], stage[:, t:t + 1, :], 0.0,
                                         still_hi[:, bass.ds(tile, 1), :].bitcast(F32),
                                         ALU.max, ALU.subtract).then_inc(still_done, 1)

            def drain(dve, ds, i, u):
                d = ds[0]
                if u.phase in ("h1a", "h1b"):
                    if d.number == units[u.phase][0].drains[0].number:
                        dve.wait_ge(biases_in, 48)
                    if u.phase == "h1b" and d.number == units["h1b"][0].drains[0].number:
                        for s in range(STAGES):
                            dve.wait_ge(stored[s], units["pass2a"][-1].drains[s].stored)
                    half = 0 if u.phase == "h1a" else BANK
                    bias = b1_rows[:, half:half + BANK]
                    if d.bank >= 2:
                        dve.wait_ge(still_done, count([q.still - 2 for q in ds], i))
                    result_done(dve, ds, i)
                    if d.tile == NT:
                        dve.tensor_tensor(rep[0:TAIL, :], ps[0:TAIL, d.bank, :], bias[0:TAIL, :], ALU.add) \
                            .then_inc(drained, 1)
                    else:
                        t = T_OF[d.bank]
                        dve.tensor_tensor(stage[:, t, :], ps[:, d.bank, :], bias, ALU.add).then_inc(drained, 1)
                    p = d.bank
                    if p > 0:
                        g = units[u.phase][u.index:u.index + len(ds)]
                        still_lo_part(g, p - 1, i)
                    return
                if u.phase == "w3":
                    if d.tile == NT:
                        result_done(dve, ds, i)
                        dve.tensor_copy(rep[0:TAIL, :], ps[0:TAIL, d.bank, :]).then_inc(drained, 1)
                        rows = slice(STEP, STEP + TAIL)
                        dve.wait_ge(still_hi_done, d.still_hi)
                        dve.tensor_tensor(still_tail[rows, :], rep[rows, :], still_tail[rows, :].bitcast(F32),
                                          ALU.subtract).then_inc(still_done, 1)
                        return
                    dve.wait_ge(still_hi_done, count([q.still_hi for q in ds], i))
                    tile = exact([q.tile for q in ds], i)
                    dve.tensor_tensor(still_lo[:, bass.ds(tile, 1), :], ps[:, d.bank:d.bank + 1, :],
                                      still_hi[:, bass.ds(tile, 1), :].bitcast(F32), ALU.subtract) \
                        .then_inc(drained, 1)
                    return
                w = u.width
                group = units[u.phase][u.index:u.index + len(ds)]
                col = exact([v.col for v in group], i)
                if u.phase != "pass1" and d.stage_free:
                    dve.wait_ge(stored[d.stage], count([q.stage_free for q in ds], i))
                result_done(dve, ds, i)
                if u.phase == "pass1":
                    dve.tensor_copy(P1[:, d.part, bass.ds(col, w)], ps[:, d.bank, 0:w]).then_inc(drained, 1)
                elif u.phase == "w2":
                    dve.tensor_scalar(stage[:, d.stage, 0:w], ps[:, d.bank, 0:w], b2_cols[:, d.part:d.part + 1], 0.0,
                                      ALU.add, ALU.max).then_inc(drained, 1)
                elif u.phase == "pass3":
                    dve.wait_ge(xT_in[d.part], count([16 * (v.index + 1) for v in group], i))
                    dve.scalar_tensor_tensor(stage[:, d.stage, 0:w], ps[:, d.bank, 0:w], b3_cols[:, d.part:d.part + 1],
                                             x_cols[:, d.part, 0:w], ALU.add, ALU.add).then_inc(drained, 1)
                else:
                    dve.tensor_copy(stage[:, d.stage, 0:w], ps[:, d.bank, 0:w]).then_inc(drained, 1)

            def finish(dve, g, i):
                if g[0].phase != "w3":
                    still_lo_part(g, len(g[0].drains) - 1, i)
                    dve.wait_ge(still_done, count([u.drains[-1].still for u in g], i))

            run_cuts_and_drains(dve, cut, drain, finish)

        @block.tensor
        def _(pe):
            def three(out, st_hi, st_lo, mv_hi, mv_lo, start, stop=False):
                pe.matmul(out, st_hi, mv_hi, start=start, stop=False)
                pe.matmul(out, st_hi, mv_lo, start=False, stop=False)
                return pe.matmul(out, st_lo, mv_hi, start=False, stop=stop)

            def bank_free(ds, i):
                need = [d.bank_free for d in ds]
                if need[-1] is None:
                    return
                pe.wait_ge(drained, count(need, i))

            def adj_chunk(us, i):
                u = us[0]
                w = u.width
                n = len(u.tiles)

                def cut_ready(t):
                    pe.wait_ge(lo_done, count([v.tiles[t].ready for v in us], i))

                def product(t, b):
                    out = ps[:, b, 0:w]
                    if t == NT:
                        return pe.matmul(out, still_tail[0:REP, b * P:(b + 1) * P], slot_tail[0:REP, 0:w],
                                         start=False, stop=True)
                    s = u.tiles[t].slot % RING
                    return three(out, still_hi[:, t, b * P:(b + 1) * P], still_lo[:, t, b * P:(b + 1) * P],
                                 slot_hi[:, s, 0:w], slot_lo[:, s, 0:w], start=t == 0)

                for t in range(n - LATE):
                    if t == 0 and u.phase != "pass1":
                        pe.wait_ge(*still_at[u.phase][0])
                    if t == n // 2 and u.phase != "pass1":
                        for wait in still_at[u.phase][1:]:
                            pe.wait_ge(*wait)
                    cut_ready(t)
                    for b in range(KF):
                        if t == 0:
                            bank_free([v.drains[b] for v in us], i)
                        mm = product(t, b)
                    mm.then_inc(slot_used, 1)
                for b in range(KF):
                    for t in range(n - LATE, n):
                        if b == 0:
                            cut_ready(t)
                        mm = product(t, b)
                        if t == n - 1:
                            mm.then_inc(acc_done, 1)
                        elif b == KF - 1:
                            mm.then_inc(slot_used, 1)

            def w2_chunk(us, i):
                u = us[0]
                w = u.width

                def product(k, m):
                    if k < RING:
                        s = u.tiles[k].slot % RING
                        hi, lo = slot_hi[:, s, 0:w], slot_lo[:, s, 0:w]
                    else:
                        hi, lo = extra_hi[:, 0:w], extra_lo[:, 0:w]
                    return three(ps[:, m, 0:w], W2_hi[:, k, m * P:(m + 1) * P], W2_lo[:, k, m * P:(m + 1) * P],
                                 hi, lo, start=k == 0, stop=k == KH - 1)

                if u.index == 0:
                    pe.wait_ge(lo_done, max(j.cut for j in units["pass2b"][-1].jobs if j.kind == "weight") + 1)
                for k in range(KH - LATE):
                    pe.wait_ge(lo_done, count([v.tiles[k].ready for v in us], i))
                    for m in range(KH):
                        if k == 0:
                            bank_free([v.drains[m] for v in us], i)
                        mm = product(k, m)
                    mm.then_inc(slot_used, 1)
                for m in range(KH):
                    for k in range(KH - LATE, KH):
                        if m == 0:
                            pe.wait_ge(lo_done, count([v.tiles[k].ready for v in us], i))
                        mm = product(k, m)
                        if k == KH - 1:
                            mm.then_inc(acc_done, 1)
                        elif m == KH - 1:
                            mm.then_inc(slot_used, 1)

            def blocks_of(us, i, positions):
                for p in positions:
                    b, bank, js, d = us[0].blocks[p]
                    bank_free([u.drains[p] for u in us], i)
                    short = b == NT
                    rows = TAIL if short else P
                    w_hi, w_lo = (W3_hi, W3_lo) if us[0].phase == "w3" else (W1_hi, W1_lo)
                    K = KH if us[0].phase == "w3" else KF
                    for k in range(K):
                        if short:
                            if k == 0:
                                pe.wait_ge(lo_done, js[0].ready)
                            hi = slot_tail[:, k * TAIL:(k + 1) * TAIL]
                            lo = slot_tail[:, BANK // 2 + k * TAIL:BANK // 2 + (k + 1) * TAIL]
                        else:
                            h, q = divmod(k, 4)
                            if q == 0:
                                pe.wait_ge(lo_done, count([u.blocks[p][2][h].ready for u in us], i))
                            s = js[h].slot % RING
                            hi = slot_hi[:, s, q * P:(q + 1) * P]
                            lo = slot_lo[:, s, q * P:(q + 1) * P]
                        mm = three(ps[0:rows, bank, :], hi, lo, w_hi[:, k, :], w_lo[:, k, :],
                                   start=k == 0, stop=k == K - 1)
                        if not short and k % 4 == 3:
                            mm.then_inc(slot_used, 1)
                    if short:
                        mm.then_inc(acc_done, 1)

            still_at = {}
            for before, name in (("h1a", "pass2a"), ("h1b", "pass2b")):
                done = units[before][-1].drains[-1].still
                still_at[name] = [(still_done, done - 3), (still_done, done)]
            y = units["w3"][-1].drains[-1]
            still_at["pass3"] = [(drained, y.number - 2), (drained, y.number), (still_done, y.still)]

            for name in order:
                us = units[name]
                if name in PASSES:
                    for g in ([us[0:1], us[1:4]] if name == "pass1" else [us[0:4]]) + [us[4:5], us[5:6]]:
                        if len(g) == 1:
                            adj_chunk(g, 0)
                        else:
                            with pe.Fori(0, len(g)) as i:
                                adj_chunk(g, i)
                elif name == "w2":
                    with pe.Fori(0, 4) as i:
                        w2_chunk(us[0:4], i)
                    w2_chunk(us[4:5], 0)
                    w2_chunk(us[5:6], 0)
                else:
                    if name == "w3":
                        w = [j for j in units["w2"][-1].jobs if j.kind == "weight"][-1].cut
                    else:
                        w = max(j.cut for j in units["pass1" if name == "h1a" else "pass2a"][4].jobs
                                if j.kind == "weight")
                    pe.wait_ge(lo_done, w + 1)
                    with pe.Fori(0, 3) as i:
                        blocks_of(us, i, range(7))
                    blocks_of(us[2:3], 0, [7])


def kernel(**inputs):
    import numpy as np
    import concourse.bacc as bacc
    from concourse.bass_utils import run_bass_kernel_spmd

    get = {k: np.asarray(v) for k, v in inputs.items()}
    x, adj = get["x"], get["adj"]
    W1, W2, W3 = (get[f"L0_gnn_W{n}"] for n in (1, 2, 3))
    b1, b2, b3 = (get[f"L0_gnn_b{n}"] for n in (1, 2, 3))
    N, F = x.shape
    H = W1.shape[1]
    arrays = {
        "x": x, "xT": x.T, "adjT": adj.T, "W1": W1, "W2": W2, "W3": W3, "b1": b1,
        "b2T": b2.reshape(-1, P).T, "b3T": b3.reshape(-1, P).T,
    }
    arrays = {k: np.ascontiguousarray(v) for k, v in arrays.items()}
    nc = bacc.Bacc("TRN2", target_bir_lowering=False, num_devices=1)
    args = [nc.dram_tensor(k, v.shape, F32, kind="ExternalInput").ap() for k, v in arrays.items()]
    outT = nc.dram_tensor("outT", (F, N), F32, kind="ExternalOutput").ap()
    P2 = nc.dram_tensor("P2", (H // P, P, N), F32, kind="Internal").ap()
    H2 = nc.dram_tensor("H2", (N // P * P, H), F32, kind="Internal").ap()
    H2tail = nc.dram_tensor("H2tail", (P, H // P, N % P), F32, kind="Internal").ap()
    gcn_kernel(nc, *args, outT, P2, H2, H2tail)
    result = run_bass_kernel_spmd(nc, [arrays], core_ids=[0])
    return np.ascontiguousarray(result.results[0]["outT"].T)
```

```python
from contextlib import ExitStack

import concourse.bass as bass
from concourse import mybir

F32 = mybir.dt.float32
F32R = mybir.dt.float32r
ALU = mybir.AluOpType
ACT = mybir.ActivationFunctionType

P = 128
BANK = 512
RING = 7
RAW = 7
HEAD = 4
LATE = 4
STAGES = 4
STEP = 32
EPS = 1e-5
CHUNK_BLOCKS = (4, 4, 4, 4, 3, 2)


def chunk_of(block):
    at = 0
    for c, n in enumerate(CHUNK_BLOCKS):
        at += n
        if block < at:
            return c
    return len(CHUNK_BLOCKS) - 1



class Job:

    def __init__(self, kind, cut, chunk=0, tile=0, col=0, width=0, half=None, source=None):
        self.kind, self.cut, self.ready = kind, cut, cut + 1
        self.chunk, self.tile, self.col, self.width, self.half, self.source = chunk, tile, col, width, half, source
        self.raw = self.raw_freed = self.tail_use = self.slot = self.acc_before = self.slot_before = None
        self.partner = None


class Drain:

    def __init__(self, number, bank, part, tile):
        self.number, self.bank, self.part, self.tile = number, bank, part, tile
        self.done = self.bank_free = self.on_slot = None
        self.stage = self.stage_free = self.stored = None
        self.still_hi = self.still = self.rep = 0


class Unit:

    def __init__(self, phase, index, col=0, width=0):
        self.phase, self.index, self.col, self.width = phase, index, col, width
        self.jobs, self.drains, self.tiles, self.blocks, self.after = [], [], [], [], []


def plan(N, F, H):
    NT, TAIL = N // P, N % P
    assert len(CHUNK_BLOCKS) * 4 >= NT and sum(CHUNK_BLOCKS) == NT
    chunks, col = [], 0
    for c, n in enumerate(CHUNK_BLOCKS):
        width = n * P + (TAIL if c == len(CHUNK_BLOCKS) - 1 else 0)
        chunks.append((col, width))
        col += width
    assert col == N and max(w for _, w in chunks) <= BANK
    now = {"cut": 0, "raw": 0, "slot": 0, "acc": 0, "drain": 0, "still_hi": 0, "still": 0, "tail": 0, "rep": 0}
    raw_user, tail_user = [None] * RAW, [None]
    stored, bank_drained = [0] * STAGES, [None] * 8
    units = {}

    def job(kind, ring=None, raw=True, **more):
        j = Job(kind, now["cut"], **more)
        now["cut"] += 1
        if raw is True:
            j.raw = now["raw"]
            before = raw_user[j.raw % RAW]
            j.raw_freed = before.cut + 1 if before else None
            raw_user[j.raw % RAW] = j
            now["raw"] += 1
        if raw == "tail":
            j.raw_freed = tail_user[0].cut + 1 if tail_user[0] else None
            tail_user[0] = j
            now["tail"] += 1
            j.tail_use = now["tail"]
        if ring:
            j.slot = now["slot"]
            now["slot"] += 1
        else:
            j.acc_before = now["acc"] or None
        return j

    def drain(bank, on_slot=None, stores=0, part=0, tile=0):
        d = Drain(now["drain"], bank, part, tile)
        d.on_slot = on_slot
        now["drain"] += 1
        if on_slot is None:
            now["acc"] += 1
            d.done = now["acc"]
        else:
            d.done = on_slot + 1
        d.bank_free = bank_drained[bank]
        bank_drained[bank] = d.number + 1
        if stores:
            d.stage = part % STAGES
            d.stage_free = 16 * stored[d.stage] or None
            stored[d.stage] += stores
            d.stored = 16 * stored[d.stage]
        return d

    def add_x(u, t):
        u.jobs.append(job("x", raw=False, tile=t))
        u.jobs[-2].ready, u.jobs[-2].partner = u.jobs[-1].ready, u.jobs[-1]

    def adj_pass(name, weights, store):
        us = []
        for c, (col, width) in enumerate(chunks):
            u = Unit(name, c, col, width)
            for t in range(NT):
                u.jobs.append(job("adj", ring=True, chunk=c, tile=t, col=col, width=width))
                if name == "pass1" and c == 0:
                    add_x(u, t)
                for w in weights.get((c, t), ()):
                    u.jobs.append(job("weight", source=w))
            u.jobs.append(job("adj", raw="tail", chunk=c, tile=NT, col=col, width=width))
            if name == "pass1" and c == 0:
                add_x(u, NT)
            u.tiles = [j for j in u.jobs if j.kind == "adj"]
            u.drains = [drain(b, part=b, stores=store) for b in range(F // P)]
            us.append(u)
        units[name] = us

    def block_phase(name, slots_per_block, blocks_per_unit=7):
        us = []
        for g in range(NT // blocks_per_unit):
            u = Unit(name, g)
            last = g == NT // blocks_per_unit - 1
            for p in range(blocks_per_unit + last):
                b = g * blocks_per_unit + p
                short = b == NT
                w = TAIL if short else P
                raw = name == "w3"
                if short:
                    js = [job(name, raw=raw, tile=b, width=w, half=None)]
                else:
                    js = [job(name, raw=raw, ring=True, tile=b, width=w, half=h) for h in range(slots_per_block)]
                u.jobs += js
                d = drain(p, on_slot=None if short else js[-1].slot, tile=b)
                now["still_hi"] += 1
                d.still_hi = now["still_hi"]
                d.rep = 0
                if short:
                    now["rep"] += 1
                    d.rep = now["rep"]
                if short or name != "w3":
                    now["still"] += 1
                d.still = now["still"]
                u.blocks.append((b, p, js, d))
                u.drains.append(d)
            us.append(u)
        units[name] = us

    def w2_phase():
        us = []
        for c, (col, width) in enumerate(chunks):
            u = Unit("w2", c, col, width)
            for k in range(H // P):
                u.tiles.append(job("p2", ring=k < RING, chunk=c, tile=k, col=col, width=width))
                u.jobs.append(u.tiles[-1])
                if c == len(chunks) - 1 and k >= HEAD:
                    for half in range(2):
                        w = job("weight", source=("W3", 2 * (k - HEAD) + half, 0))
                        w.acc_before, w.slot_before = None, u.tiles[k - HEAD].slot + 1
                        u.jobs.append(w)
            u.drains = [drain(m, part=m, stores=2 if width % P else 1) for m in range(H // P)]
            us.append(u)
        units["w2"] = us

    KF, KH = F // P, H // P
    adj_pass("pass1", {(4, 5 + 2 * k): [("W1", k, 0)] for k in range(KF)}, 0)
    block_phase("h1a", 1)
    adj_pass("pass2a", {(4, 5 + 2 * k): [("W1", k, 1)] for k in range(KF)}, 1)
    block_phase("h1b", 1)
    adj_pass("pass2b", {(4, 4 + k): [("W2", k // 2, k % 2)] for k in range(2 * KH)}, 1)
    w2_phase()
    block_phase("w3", 2)
    adj_pass("pass3", {}, 1)
    order = ["pass1", "h1a", "pass2a", "h1b", "pass2b", "w2", "w3", "pass3"]
    flat = [u for name in order for u in units[name]]
    for u, v in zip(flat, flat[1:]):
        u.after = v.jobs
    flat[-1].after = []
    return units, order, [16 * s for s in stored]


def exact(values, i):
    step = values[1] - values[0] if len(values) > 1 else 0
    assert all(v == values[0] + k * step for k, v in enumerate(values))
    return values[0] + i * step if step else values[0]


def count(values, i):
    step = values[-1] - values[-2] if len(values) > 1 else 0
    least = max(v - k * step for k, v in enumerate(values) if v is not None)
    assert least > 0
    return least + i * step if step else least


def gcn_kernel(nc, x, xT, adjT, W1, W2, W3, b1, b2T, b3T, outT, P2, H2, H2tail):
    N, F = x.shape
    H = W1.shape[1]
    NT, TAIL = N // P, N % P
    KF, KH = F // P, H // P
    REP = 2 * STEP + TAIL
    LO_AT = KH * TAIL + STEP
    assert LO_AT + (KH - 1) * TAIL + P <= BANK
    units, order, stored_all = plan(N, F, H)
    PASSES = ("pass1", "pass2a", "pass2b", "pass3")

    at = nc.sbuf_base + (-nc.sbuf_base) % 64

    def place(name, shape, dtype, offset=None):
        nonlocal at
        here = at if offset is None else offset
        size = 4
        for n in shape[1:]:
            size *= n
        if offset is None:
            at += size + (-size) % 64
        assert here + size <= nc.sbuf_usable_end
        return nc.alloc_sbuf_tensor_at(name, shape, dtype, offset=here)

    still_hi = place("still_hi", [P, NT, F], F32R)
    still_lo = place("still_lo", [P, NT, F], F32R)
    still_tail = place("still_tail", [P, F], F32R)
    slot_hi = place("slot_hi", [P, RING, BANK], F32R)
    slot_lo = place("slot_lo", [P, RING, BANK], F32R)
    slot_tail = place("slot_tail", [P, BANK], F32R)
    raw = place("raw", [P, RAW, BANK], F32)
    raw_tail = place("raw_tail", [P, BANK], F32)
    stage = place("stage", [P, STAGES, BANK], F32)
    rep = place("rep", [P, F], F32)
    b2_cols = place("b2_cols", [P, KH], F32)
    b3_cols = place("b3_cols", [P, KF], F32)
    stats = place("stats", [P, 6 * 2], F32)
    moments = place("moments", [P, 2 * (NT + 1)], F32)
    spread = place("spread", [P, 7 * (NT + 1)], F32)
    region = at
    P1 = place("P1", [P, KF, N], F32)
    W1_hi = place("W1_hi", [P, KF, BANK], F32R)
    W1_lo = place("W1_lo", [P, KF, BANK], F32R)
    b1_rows = place("b1_rows", [P, H], F32)
    W2_hi = place("W2_hi", [P, KH, H], F32R, region)
    W2_lo = place("W2_lo", [P, KH, H], F32R, region + KH * H * 4)
    W3_hi = place("W3_hi", [P, KH, F], F32R, region)
    W3_lo = place("W3_lo", [P, KH, F], F32R, region + KH * H * 4)
    x_cols = place("x_cols", [P, KF, BANK], F32, region)
    extra_hi = still_hi[:, NT - 1, :]
    extra_lo = still_lo[:, NT - 1, :]

    with ExitStack() as ctx:
        def sem(name):
            return ctx.enter_context(nc.semaphore(name))

        ps = ctx.enter_context(nc.psum_tensor("ps", [P, 8, BANK], F32))

        zeroed = sem("zeroed")
        rep_zeroed = sem("rep_zeroed")
        biases_in = sem("biases_in")
        raw_in = [sem(f"raw_in{r}") for r in range(RAW)]
        tail_in = sem("tail_in")
        x_in = [sem(f"x_in{s}") for s in range(STAGES)]
        xT_in = [sem(f"xT_in{b}") for b in range(KF)]
        rep_in = sem("rep_in")
        table_loaded = sem("table_loaded")
        stats_done = sem("stats_done")
        moments_done = sem("moments_done")
        shift_done = sem("shift_done")
        root_done = sem("root_done")
        centred = sem("centred")
        inverse_done = sem("inverse_done")
        newton_done = sem("newton_done")
        hi_done = sem("hi_done")
        lo_done = sem("lo_done")
        slot_used = sem("slot_used")
        acc_done = sem("acc_done")
        drained = sem("drained")
        still_hi_done = sem("still_hi_done")
        still_done = sem("still_done")
        stored = [sem(f"stored{s}") for s in range(STAGES)]

        block = ctx.enter_context(nc.Block())

        def cut_parts(js):
            j = js[0]
            if j.kind == "weight":
                name, k, half = j.source
                cols = slice(half * BANK, half * BANK + BANK) if name == "W2" else slice(0, BANK)
                hi, lo = {"W1": (W1_hi, W1_lo), "W2": (W2_hi, W2_lo), "W3": (W3_hi, W3_lo)}[name]
                return hi[:, k, cols], lo[:, k, cols], raw[:, j.raw % RAW, :]
            if j.kind == "h1a" or j.kind == "h1b":
                if j.slot is None:
                    w = KF * TAIL
                    return (slot_tail[:, 0:w].rearrange("p (k i) -> p k i", k=KF),
                            slot_tail[:, LO_AT:LO_AT + w].rearrange("p (k i) -> p k i", k=KF),
                            P1[:, :, NT * P:N])
                return (slot_hi[:, j.slot % RING, :].rearrange("p (k i) -> p k i", k=KF),
                        slot_lo[:, j.slot % RING, :].rearrange("p (k i) -> p k i", k=KF), None)
            if j.kind == "w3" and j.slot is None:
                w = KH * TAIL
                return slot_tail[:, 0:w], slot_tail[:, LO_AT:LO_AT + w], raw[:, j.raw % RAW, 0:w]
            if j.kind == "w3":
                return slot_hi[:, j.slot % RING, :], slot_lo[:, j.slot % RING, :], raw[:, j.raw % RAW, :]
            w = j.width
            if j.kind == "p2" and j.slot is None:
                return extra_hi[:, 0:w], extra_lo[:, 0:w], raw[:, j.raw % RAW, 0:w]
            return slot_hi[:, j.slot % RING, 0:w], slot_lo[:, j.slot % RING, 0:w], raw[:, j.raw % RAW, 0:w]

        def source_of(js, i):
            hi, lo, src = cut_parts(js)
            if src is None:
                src = P1[:, :, bass.ds(exact([j.tile for j in js], i) * P, P)]
            return hi, lo, src

        x_jobs = [j for j in units["pass1"][0].jobs if j.kind == "x"]

        def x_tile(t):
            return (rep[0:REP, :], slice(0, REP)) if t == NT else (stage[:, t % STAGES, :], slice(0, P))

        def x_column(t, which):
            rows = slice(0, REP if t == NT else P)
            k = ("-mean", "v", "root", "r", "vrr", "step", "scale").index(which)
            return spread[rows, 7 * t + k:7 * t + k + 1]

        @block.sync
        def _(sp):
            def load(js, i):
                j = js[0]
                if j.kind in ("h1a", "h1b"):
                    return
                if j.kind == "x" and j.tile == NT:
                    for r in range(3):
                        sp.dma_start(rep[r * STEP:r * STEP + TAIL, :], x[NT * P:N, :]).then_inc(rep_in, 16)
                    return
                if j.kind == "x":
                    s = j.tile % STAGES
                    if j.tile >= STAGES:
                        sp.wait_ge(lo_done, x_jobs[j.tile - STAGES].cut + 1)
                    sp.dma_start(stage[:, s, :], x[j.tile * P:(j.tile + 1) * P, :]).then_inc(x_in[s], 16)
                    return
                if j.raw_freed is not None:
                    sp.wait_ge(lo_done, count([q.raw_freed for q in js], i))
                if j.tail_use is not None:
                    src = adjT[NT * P:N, bass.ds(exact([q.col for q in js], i), j.width)]
                    for r in range(3):
                        sp.dma_start(raw_tail[r * STEP:r * STEP + TAIL, 0:j.width], src).then_inc(tail_in, 16)
                    return
                r = j.raw % RAW
                if j.kind == "weight":
                    name, k, half = j.source
                    w = {"W1": W1, "W2": W2, "W3": W3}[name]
                    sp.dma_start(raw[:, r, :], w[k * P:(k + 1) * P, half * BANK:half * BANK + BANK]) \
                        .then_inc(raw_in[r], 16)
                elif j.kind == "adj":
                    sp.dma_start(raw[:, r, 0:j.width],
                                 adjT[j.tile * P:(j.tile + 1) * P, bass.ds(exact([q.col for q in js], i), j.width)]) \
                        .then_inc(raw_in[r], 16)
                elif j.kind == "p2":
                    made = [units["pass2a" if q.tile < KF else "pass2b"][q.chunk].drains[q.tile % KF] for q in js]
                    sp.wait_ge(stored[made[0].stage], count([d.stored for d in made], i))
                    sp.dma_start(raw[:, r, 0:j.width], P2[j.tile, :, bass.ds(exact([q.col for q in js], i), j.width)]) \
                        .then_inc(raw_in[r], 16)
                elif j.slot is None:
                    for s in range(STAGES):
                        sp.wait_ge(stored[s], units["w2"][-1].drains[KH - STAGES + s].stored)
                    sp.dma_start(raw[:, r, 0:KH * TAIL], H2tail.rearrange("p k i -> p (k i)")).then_inc(raw_in[r], 16)
                else:
                    made = [units["w2"][chunk_of(q.tile)] for q in js]
                    for s in range(STAGES):
                        sp.wait_ge(stored[s], max(u.drains[KH - STAGES + s].stored for u in made))
                    b = exact([q.tile for q in js], i)
                    half = KH // 2 * P
                    sp.dma_start(raw[:, r, :], H2[bass.ds(b * P, P), j.half * half:(j.half + 1) * half]) \
                        .then_inc(raw_in[r], 16)

            def load_xT(us, i):
                for b in range(KF):
                    if us[0].index == 0:
                        sp.wait_ge(acc_done, units["w3"][-1].drains[-1].done)
                    else:
                        sp.wait_ge(drained, count([units["pass3"][u.index - 1].drains[b].number + 1 for u in us], i))
                    sp.dma_start(x_cols[:, b, 0:us[0].width],
                                 xT[b * P:(b + 1) * P, bass.ds(exact([u.col for u in us], i), us[0].width)]) \
                        .then_inc(xT_in[b], 16)

            def unit_loads(us, i):
                for q, j in enumerate(us[0].jobs):
                    if us[0].phase == "pass3" and q == 12:
                        load_xT(us, i)
                    load([u.jobs[q] for u in us], i)

            for j in units["pass1"][0].jobs:
                if j.partner is not None:
                    if j.tile == 1:
                        sp.wait_ge(rep_zeroed, 1)
                        sp.wait_ge(zeroed, 2)
                    load([j.partner], 0)
                    load([j], 0)
            sp.dma_start(b1_rows[:, :], b1.partition_broadcast(P)).then_inc(biases_in, 16)
            sp.dma_start(b2_cols[:, :], b2T).then_inc(biases_in, 16)
            sp.dma_start(b3_cols[:, :], b3T).then_inc(biases_in, 16)
            for name in order:
                us = units[name]
                if name in ("h1a", "h1b"):
                    continue
                if name == "pass1":
                    groups = [us[1:4], us[4:5], us[5:6]]
                elif name == "pass3":
                    groups = [us[0:1], us[1:4], us[4:5], us[5:6]]
                elif name == "w3":
                    groups = [us[0:2], us[2:3]]
                elif name == "w2":
                    groups = [[u] for u in us]
                else:
                    groups = [us[0:4], us[4:5], us[5:6]]
                for g in groups:
                    if len(g) == 1:
                        unit_loads(g, 0)
                    else:
                        with sp.Fori(0, len(g)) as i:
                            unit_loads(g, i)
            for s in range(STAGES):
                sp.wait_ge(stored[s], stored_all[s])

        def cut_hi(act, js, i):
            j = js[0]
            if j.kind == "x":
                act.wait_ge(newton_done, 3 * (j.tile + 1))
                tile, rows = x_tile(j.tile)
                hi = still_tail[rows, :] if j.tile == NT else still_hi[:, j.tile, :]
                act.activation(hi, tile, ACT.Relu, scale=x_column(j.tile, "scale")).then_inc(hi_done, 1)
                return
            if j.raw is not None:
                act.wait_ge(raw_in[j.raw % RAW], count([16 * (q.raw // RAW + 1) for q in js], i))
            if j.tail_use is not None:
                act.wait_ge(tail_in, count([48 * q.tail_use for q in js], i))
            if j.slot is not None and j.slot >= RING:
                act.wait_ge(slot_used, count([q.slot - RING + 1 for q in js], i))
            elif j.kind == "weight" and j.source[0] == "W3":
                act.wait_ge(slot_used, j.slot_before)
            elif j.acc_before is not None:
                act.wait_ge(acc_done, count([q.acc_before for q in js], i))
            if j.kind in ("h1a", "h1b"):
                act.wait_ge(drained, max(units["pass1"][chunk_of(q.tile)].drains[-1].number + 1 for q in js))
            if j.kind == "adj" and j.tail_use is not None:
                act.copy(slot_tail[0:REP, 0:j.width], raw_tail[0:REP, 0:j.width]).then_inc(hi_done, 1)
                return
            hi, lo, src = source_of(js, i)
            act.copy(hi, src).then_inc(hi_done, 1)

        def cut_lo(dve, js, i):
            j = js[0]
            dve.wait_ge(hi_done, count([q.cut + 1 for q in js], i))
            if j.kind == "x":
                tile, rows = x_tile(j.tile)
                scale, hi, lo = x_column(j.tile, "scale"), still_hi[:, j.tile % NT, :], still_lo[:, j.tile % NT, :]
                if j.tile == NT:
                    rows = slice(STEP, STEP + TAIL)
                    tile, hi, lo = rep[rows, :], still_tail[rows, :], still_tail[rows, :]
                    scale = spread[rows, 7 * NT + 6:7 * NT + 7]
                dve.scalar_tensor_tensor(lo, tile, scale, hi.bitcast(F32), ALU.mult, ALU.subtract) \
                    .then_inc(lo_done, 1)
            elif j.kind == "adj" and j.tail_use is not None:
                rows = slice(2 * STEP, REP)
                dve.tensor_tensor(slot_tail[rows, 0:j.width], raw_tail[rows, 0:j.width],
                                  slot_tail[rows, 0:j.width].bitcast(F32), ALU.subtract).then_inc(lo_done, 1)
            else:
                hi, lo, src = source_of(js, i)
                dve.tensor_tensor(lo, src, hi.bitcast(F32), ALU.subtract).then_inc(lo_done, 1)

        def chunk_groups(name, us):
            if name == "w2":
                return [[u] for u in us]
            if name == "pass2b":
                return [us[0:3], us[3:4], us[4:5], us[5:6]]
            return [us[0:1], us[1:3], us[3:4], us[4:5], us[5:6]]

        def ahead(us, q):
            return [(u.jobs + u.after)[q] if q < len(u.jobs) + len(u.after) else None for u in us]

        def run_cuts_and_drains(eng, cut, drain, finish, drain_first=()):
            for name in order:
                us = units[name]
                if name in PASSES or name == "w2":
                    for g in chunk_groups(name, us):
                        def body(i):
                            n = len(g[0].jobs)
                            begin = 0 if (name == "pass1" and g[0].index == 0) else HEAD
                            for q in range(begin, n + (HEAD if g[0].after else 0)):
                                cut(eng, ahead(g, q), i)
                            for b in range(len(g[0].drains)):
                                drain(eng, [u.drains[b] for u in g], i, g[0])
                        if len(g) == 1:
                            body(0)
                        else:
                            with eng.Fori(0, len(g)) as i:
                                body(i)
                else:
                    per = 2 if name == "w3" else 1
                    for g in (us[0:2], us[2:3]):
                        def body(i):
                            q = HEAD
                            n = len(g[0].jobs)
                            nb = len(g[0].blocks)
                            for p in range(nb):
                                upto = n + HEAD if p == nb - 1 else min(HEAD + per * (p + 1), n + HEAD)
                                first = name in drain_first and p == nb - 1
                                if first:
                                    drain(eng, [u.drains[p] for u in g], i, g[0])
                                while q < upto:
                                    cut(eng, ahead(g, q), i)
                                    q += 1
                                if not first:
                                    drain(eng, [u.drains[p] for u in g], i, g[0])
                            finish(eng, g, i)
                        if len(g) == 1:
                            body(0)
                        else:
                            with eng.Fori(0, len(g)) as i:
                                body(i)

        def result_done(eng, ds, i):
            eng.wait_ge(acc_done if ds[0].on_slot is None else slot_used, count([d.done for d in ds], i))

        T_OF = [0, 1, 0, 1, 0, 1, 2]

        @block.scalar
        def _(act):
            def drain(act, ds, i, u):
                d = ds[0]
                if u.phase == "pass1":
                    return
                if u.phase in ("h1a", "h1b", "w3"):
                    short = d.tile == NT
                    if short:
                        act.wait_ge(drained, d.number + 1)
                        for r in (1, 2):
                            act.dma_start(rep[r * STEP:r * STEP + TAIL, :], rep[0:TAIL, :]).then_inc(rep_in, 16)
                        act.wait_ge(rep_in, 48 + 32 * d.rep)
                        act.activation(still_tail[0:REP, :], rep[0:REP, :],
                                       ACT.Copy if u.phase == "w3" else ACT.Relu).then_inc(still_hi_done, 1)
                        return
                    tile = exact([q.tile for q in ds], i)
                    if u.phase == "w3":
                        result_done(act, ds, i)
                        act.copy(still_hi[:, bass.ds(tile, 1), :], ps[:, d.bank:d.bank + 1, :]) \
                            .then_inc(still_hi_done, 1)
                    else:
                        act.wait_ge(drained, count([q.number + 1 for q in ds], i))
                        t = T_OF[d.bank]
                        act.activation(still_hi[:, bass.ds(tile, 1), :], stage[:, t:t + 1, :], ACT.Relu) \
                            .then_inc(still_hi_done, 1)
                    return
                act.wait_ge(drained, count([q.number + 1 for q in ds], i))
                w = u.width
                group = units[u.phase][u.index:u.index + len(ds)]
                col = exact([v.col for v in group], i)
                s = d.stage
                if u.phase == "pass3":
                    act.dma_start(outT[d.part * P:(d.part + 1) * P, bass.ds(col, w)], stage[:, s, 0:w]) \
                        .then_inc(stored[s], 16)
                elif u.phase == "w2":
                    full = w // P
                    b0 = u.col // P
                    act.dma_start(H2[b0 * P:(b0 + full) * P, d.part * P:(d.part + 1) * P]
                                  .rearrange("(b p) i -> p b i", p=P),
                                  stage[:, s, 0:full * P].rearrange("p (b i) -> p b i", i=P)).then_inc(stored[s], 16)
                    if w % P:
                        act.dma_start(H2tail[:, d.part, :], stage[:, s, full * P:w]).then_inc(stored[s], 16)
                else:
                    k = d.part + (KF if u.phase == "pass2b" else 0)
                    act.dma_start(P2[k, :, bass.ds(col, w)], stage[:, s, 0:w]).then_inc(stored[s], 16)

            act.wait_ge(rep_zeroed, 1)
            act.activation(spread[0:1, 0:1], rep[0:1, 0:1], ACT.Sqrt).then_inc(table_loaded, 1)

            def root(t):
                act.wait_ge(shift_done, 2 * (t + 1))
                act.activation(x_column(t, "root"), x_column(t, "v"), ACT.Sqrt).then_inc(root_done, 1)

            def centre(t):
                tile, rows = x_tile(t)
                act.activation(tile, tile, ACT.Relu, bias=x_column(t, "-mean")).then_inc(centred, 1)

            def cut(act, js, i):
                j = js[0]
                if j.kind == "x" and j.tile == 0:
                    root(0)
                    centre(0)
                    root(1)
                if j.kind == "x":
                    act.wait_ge(centred, j.tile + 1)
                cut_hi(act, js, i)
                if j.kind == "x" and j.tile + 2 <= NT:
                    root(j.tile + 2)
                if j.kind == "x" and j.tile + 1 <= NT:
                    centre(j.tile + 1)

            run_cuts_and_drains(act, cut, drain, lambda *a: None)

        @block.vector
        def _(dve):
            dve.memset(rep[:, :], 0.0).then_inc(rep_zeroed, 1)
            dve.memset(raw_tail[:, :], 0.0).then_inc(zeroed, 1)

            def statistics(t):
                tile, rows = x_tile(t)
                if t == NT:
                    dve.wait_ge(rep_in, 48)
                else:
                    dve.wait_ge(x_in[t % STAGES], 16 * (t // STAGES + 1))
                half = 6 * (t % 2)
                dve.bn_stats(stats[rows, half:half + 6], tile).then_inc(stats_done, 1)
                dve.wait_ge(stats_done, t + 1)
                dve.bn_aggr(moments[rows, 2 * t:2 * t + 2], stats[rows, half:half + 6]).then_inc(moments_done, 1)

            def inverse(t):
                dve.wait_ge(root_done, t + 1)
                dve.reciprocal(x_column(t, "r"), x_column(t, "root")).then_inc(inverse_done, 1)

            def cut(dve, js, i):
                j = js[0]
                if j.partner is not None:
                    t = j.partner.tile
                    if t == 0:
                        statistics(0)
                        inverse(0)
                        statistics(1)
                    elif t + 2 <= NT:
                        statistics(t + 2)
                    if t + 1 <= NT:
                        inverse(t + 1)
                cut_lo(dve, js, i)
                if j.kind == "x" and j.tile == 0:
                    statistics(2)

            def still_lo_part(g, p, i):
                ds = [u.drains[p] for u in g]
                d = ds[0]
                dve.wait_ge(still_hi_done, count([q.still_hi for q in ds], i))
                if d.tile == NT:
                    rows = slice(STEP, STEP + TAIL)
                    dve.scalar_tensor_tensor(still_tail[rows, :], rep[rows, :], 0.0, still_tail[rows, :].bitcast(F32),
                                             ALU.max, ALU.subtract).then_inc(still_done, 1)
                    return
                tile = exact([q.tile for q in ds], i)
                t = T_OF[d.bank]
                dve.scalar_tensor_tensor(still_lo[:, bass.ds(tile, 1), :], stage[:, t:t + 1, :], 0.0,
                                         still_hi[:, bass.ds(tile, 1), :].bitcast(F32),
                                         ALU.max, ALU.subtract).then_inc(still_done, 1)

            def drain(dve, ds, i, u):
                d = ds[0]
                if u.phase in ("h1a", "h1b"):
                    if d.number == units[u.phase][0].drains[0].number:
                        dve.wait_ge(biases_in, 48)
                    if u.phase == "h1b" and d.number == units["h1b"][0].drains[0].number:
                        for s in range(STAGES):
                            dve.wait_ge(stored[s], units["pass2a"][-1].drains[s].stored)
                    half = 0 if u.phase == "h1a" else BANK
                    bias = b1_rows[:, half:half + BANK]
                    if d.bank >= 2:
                        dve.wait_ge(still_done, count([q.still - 2 for q in ds], i))
                    result_done(dve, ds, i)
                    if d.tile == NT:
                        dve.tensor_tensor(rep[0:TAIL, :], ps[0:TAIL, d.bank, :], bias[0:TAIL, :], ALU.add) \
                            .then_inc(drained, 1)
                    else:
                        t = T_OF[d.bank]
                        dve.tensor_tensor(stage[:, t, :], ps[:, d.bank, :], bias, ALU.add).then_inc(drained, 1)
                    p = d.bank
                    if p > 0:
                        g = units[u.phase][u.index:u.index + len(ds)]
                        still_lo_part(g, p - 1, i)
                    return
                if u.phase == "w3":
                    if d.tile == NT:
                        result_done(dve, ds, i)
                        dve.tensor_copy(rep[0:TAIL, :], ps[0:TAIL, d.bank, :]).then_inc(drained, 1)
                        rows = slice(STEP, STEP + TAIL)
                        dve.wait_ge(still_hi_done, d.still_hi)
                        dve.tensor_tensor(still_tail[rows, :], rep[rows, :], still_tail[rows, :].bitcast(F32),
                                          ALU.subtract).then_inc(still_done, 1)
                        return
                    dve.wait_ge(still_hi_done, count([q.still_hi for q in ds], i))
                    tile = exact([q.tile for q in ds], i)
                    dve.tensor_tensor(still_lo[:, bass.ds(tile, 1), :], ps[:, d.bank:d.bank + 1, :],
                                      still_hi[:, bass.ds(tile, 1), :].bitcast(F32), ALU.subtract) \
                        .then_inc(drained, 1)
                    return
                w = u.width
                group = units[u.phase][u.index:u.index + len(ds)]
                col = exact([v.col for v in group], i)
                if d.stage_free:
                    dve.wait_ge(stored[d.stage], count([q.stage_free for q in ds], i))
                result_done(dve, ds, i)
                if u.phase == "pass1":
                    dve.tensor_copy(P1[:, d.part, bass.ds(col, w)], ps[:, d.bank, 0:w]).then_inc(drained, 1)
                elif u.phase == "w2":
                    dve.tensor_scalar(stage[:, d.stage, 0:w], ps[:, d.bank, 0:w], b2_cols[:, d.part:d.part + 1], 0.0,
                                      ALU.add, ALU.max).then_inc(drained, 1)
                elif u.phase == "pass3":
                    dve.wait_ge(xT_in[d.part], count([16 * (v.index + 1) for v in group], i))
                    dve.scalar_tensor_tensor(stage[:, d.stage, 0:w], ps[:, d.bank, 0:w], b3_cols[:, d.part:d.part + 1],
                                             x_cols[:, d.part, 0:w], ALU.add, ALU.add).then_inc(drained, 1)
                else:
                    dve.tensor_copy(stage[:, d.stage, 0:w], ps[:, d.bank, 0:w]).then_inc(drained, 1)

            def finish(dve, g, i):
                if g[0].phase != "w3":
                    still_lo_part(g, len(g[0].drains) - 1, i)
                    dve.wait_ge(still_done, count([u.drains[-1].still for u in g], i))

            run_cuts_and_drains(dve, cut, drain, finish, drain_first=("h1a", "h1b"))

        @block.gpsimd
        def _(pool):
            def shifts(t):
                rows = slice(0, REP if t == NT else P)
                pool.wait_ge(moments_done, t + 1)
                pool.tensor_scalar(x_column(t, "v"), moments[rows, 2 * t + 1:2 * t + 2], EPS, None, ALU.add) \
                    .then_inc(shift_done, 1)
                pool.tensor_scalar(x_column(t, "-mean"), moments[rows, 2 * t:2 * t + 1], -1.0, None, ALU.mult) \
                    .then_inc(shift_done, 1)

            def newton(t):
                v, r, vrr, step, scale = (x_column(t, k) for k in ("v", "r", "vrr", "step", "scale"))
                pool.wait_ge(inverse_done, t + 1)
                pool.tensor_scalar(vrr, v, r, r, ALU.mult, ALU.mult).then_inc(newton_done, 1)
                pool.wait_ge(newton_done, 3 * t + 1)
                pool.tensor_scalar(step, vrr, -0.5, 1.5, ALU.mult, ALU.add).then_inc(newton_done, 1)
                pool.wait_ge(newton_done, 3 * t + 2)
                pool.tensor_tensor(scale, step, r, ALU.mult).then_inc(newton_done, 1)

            pool.memset(slot_tail[:, :].bitcast(F32), 0.0).then_inc(zeroed, 1)
            pool.wait_ge(table_loaded, 1)
            shifts(0)
            newton(0)
            shifts(1)
            for t in range(NT + 1):
                if t + 2 <= NT:
                    shifts(t + 2)
                if t + 1 <= NT:
                    newton(t + 1)

        @block.tensor
        def _(pe):
            def three(out, st_hi, st_lo, mv_hi, mv_lo, start, stop=False):
                pe.matmul(out, st_hi, mv_hi, start=start, stop=False)
                pe.matmul(out, st_hi, mv_lo, start=False, stop=False)
                return pe.matmul(out, st_lo, mv_hi, start=False, stop=stop)

            def bank_free(ds, i):
                need = [d.bank_free for d in ds]
                if need[-1] is None:
                    return
                pe.wait_ge(drained, count(need, i))

            def adj_chunk(us, i):
                u = us[0]
                w = u.width
                n = len(u.tiles)

                def cut_ready(t):
                    pe.wait_ge(lo_done, count([v.tiles[t].ready for v in us], i))

                def product(t, b):
                    out = ps[:, b, 0:w]
                    if t == NT:
                        return pe.matmul(out, still_tail[0:REP, b * P:(b + 1) * P], slot_tail[0:REP, 0:w],
                                         start=False, stop=True)
                    s = u.tiles[t].slot % RING
                    return three(out, still_hi[:, t, b * P:(b + 1) * P], still_lo[:, t, b * P:(b + 1) * P],
                                 slot_hi[:, s, 0:w], slot_lo[:, s, 0:w], start=t == 0)

                for t in range(n - LATE):
                    if t == 0 and u.phase != "pass1":
                        pe.wait_ge(*still_at[u.phase][0])
                    if t == n // 2 and u.phase != "pass1":
                        for wait in still_at[u.phase][1:]:
                            pe.wait_ge(*wait)
                    cut_ready(t)
                    for b in range(KF):
                        if t == 0:
                            bank_free([v.drains[b] for v in us], i)
                        mm = product(t, b)
                    mm.then_inc(slot_used, 1)
                for b in range(KF):
                    for t in range(n - LATE, n):
                        if b == 0:
                            cut_ready(t)
                        mm = product(t, b)
                        if t == n - 1:
                            mm.then_inc(acc_done, 1)
                        elif b == KF - 1:
                            mm.then_inc(slot_used, 1)

            def w2_chunk(us, i):
                u = us[0]
                w = u.width

                def product(k, m):
                    if k < RING:
                        s = u.tiles[k].slot % RING
                        hi, lo = slot_hi[:, s, 0:w], slot_lo[:, s, 0:w]
                    else:
                        hi, lo = extra_hi[:, 0:w], extra_lo[:, 0:w]
                    return three(ps[:, m, 0:w], W2_hi[:, k, m * P:(m + 1) * P], W2_lo[:, k, m * P:(m + 1) * P],
                                 hi, lo, start=k == 0, stop=k == KH - 1)

                if u.index == 0:
                    pe.wait_ge(lo_done, max(j.cut for j in units["pass2b"][4].jobs if j.kind == "weight") + 1)
                for k in range(KH - LATE):
                    pe.wait_ge(lo_done, count([v.tiles[k].ready for v in us], i))
                    for m in range(KH):
                        if k == 0:
                            bank_free([v.drains[m] for v in us], i)
                        mm = product(k, m)
                    mm.then_inc(slot_used, 1)
                for m in range(KH):
                    for k in range(KH - LATE, KH):
                        if m == 0:
                            pe.wait_ge(lo_done, count([v.tiles[k].ready for v in us], i))
                        mm = product(k, m)
                        if k == KH - 1:
                            mm.then_inc(acc_done, 1)
                        elif m == KH - 1:
                            mm.then_inc(slot_used, 1)

            def blocks_of(us, i, positions):
                for p in positions:
                    b, bank, js, d = us[0].blocks[p]
                    bank_free([u.drains[p] for u in us], i)
                    short = b == NT
                    w_hi, w_lo = (W3_hi, W3_lo) if us[0].phase == "w3" else (W1_hi, W1_lo)
                    K = KH if us[0].phase == "w3" else KF
                    for k in range(K):
                        if short:
                            if k == 0:
                                pe.wait_ge(lo_done, js[0].ready)
                            hi = slot_tail[:, k * TAIL:k * TAIL + P]
                            lo = slot_tail[:, LO_AT + k * TAIL:LO_AT + k * TAIL + P]
                        else:
                            h, q = divmod(k, 4)
                            if q == 0:
                                pe.wait_ge(lo_done, count([u.blocks[p][2][h].ready for u in us], i))
                            s = js[h].slot % RING
                            hi = slot_hi[:, s, q * P:(q + 1) * P]
                            lo = slot_lo[:, s, q * P:(q + 1) * P]
                        mm = three(ps[:, bank, :], hi, lo, w_hi[:, k, :], w_lo[:, k, :],
                                   start=k == 0, stop=k == K - 1)
                        if not short and k % 4 == 3:
                            mm.then_inc(slot_used, 1)
                    if short:
                        mm.then_inc(acc_done, 1)

            still_at = {}
            for before, name in (("h1a", "pass2a"), ("h1b", "pass2b")):
                done = units[before][-1].drains[-1].still
                still_at[name] = [(still_done, done - (NT + 1) // 2 + 1), (still_done, done)]
            y = units["w3"][-1].drains[-1]
            still_at["pass3"] = [(drained, y.number + 1 - (NT + 1) // 2 + 1), (drained, y.number), (still_done, y.still)]

            for name in order:
                us = units[name]
                if name in PASSES:
                    for g in ([us[0:1], us[1:4]] if name == "pass1" else [us[0:4]]) + [us[4:5], us[5:6]]:
                        if len(g) == 1:
                            adj_chunk(g, 0)
                        else:
                            with pe.Fori(0, len(g)) as i:
                                adj_chunk(g, i)
                elif name == "w2":
                    with pe.Fori(0, 4) as i:
                        w2_chunk(us[0:4], i)
                    w2_chunk(us[4:5], 0)
                    w2_chunk(us[5:6], 0)
                else:
                    if name == "w3":
                        w = [j for j in units["w2"][-1].jobs if j.kind == "weight"][-1].cut
                    else:
                        w = max(j.cut for j in units["pass1" if name == "h1a" else "pass2a"][4].jobs
                                if j.kind == "weight")
                    pe.wait_ge(lo_done, w + 1)
                    with pe.Fori(0, 3) as i:
                        blocks_of(us, i, range(7))
                    blocks_of(us[2:3], 0, [7])


def kernel(**inputs):
    import numpy as np
    import concourse.bacc as bacc
    from concourse.bass_utils import run_bass_kernel_spmd

    get = {k: np.asarray(v) for k, v in inputs.items()}
    x, adj = get["x"], get["adj"]
    W1, W2, W3 = (get[f"L0_gnn_W{n}"] for n in (1, 2, 3))
    b1, b2, b3 = (get[f"L0_gnn_b{n}"] for n in (1, 2, 3))
    N, F = x.shape
    H = W1.shape[1]
    arrays = {
        "x": x, "xT": x.T, "adjT": adj.T, "W1": W1, "W2": W2, "W3": W3, "b1": b1,
        "b2T": b2.reshape(-1, P).T, "b3T": b3.reshape(-1, P).T,
    }
    arrays = {k: np.ascontiguousarray(v) for k, v in arrays.items()}
    nc = bacc.Bacc("TRN2", target_bir_lowering=False, num_devices=1)
    args = [nc.dram_tensor(k, v.shape, F32, kind="ExternalInput").ap() for k, v in arrays.items()]
    outT = nc.dram_tensor("outT", (F, N), F32, kind="ExternalOutput").ap()
    P2 = nc.dram_tensor("P2", (H // P, P, N), F32, kind="Internal").ap()
    H2 = nc.dram_tensor("H2", (N // P * P, H), F32, kind="Internal").ap()
    H2tail = nc.dram_tensor("H2tail", (P, H // P, N % P), F32, kind="Internal").ap()
    gcn_kernel(nc, *args, outT, P2, H2, H2tail)
    result = run_bass_kernel_spmd(nc, [arrays], core_ids=[0])
    return np.ascontiguousarray(result.results[0]["outT"].T)
```
